# Optimizing a Trainium2 kernel written in Bass

```python
import numpy as np
import jax
import jax.numpy as jnp

def _softmax(x, axis=-1):
    return jax.nn.softmax(x, axis=axis)

def _gelu(x):
    return jax.nn.gelu(x, approximate=True)

def _silu(x):
    return jax.nn.silu(x)

def _sigmoid(x):
    return jax.nn.sigmoid(x)

def _layernorm(x, axis=-1, eps=1e-05):
    m = jnp.mean(x, axis=axis, keepdims=True)
    v = jnp.var(x, axis=axis, keepdims=True)
    return (x - m) / jnp.sqrt(v + eps)

def _scatter_add(tgt, idx, src, axis=0):
    return tgt.at[idx].add(src)

def _segment_sum(src, seg, n):
    return jax.ops.segment_sum(src, seg, n)
kernel_name = 'mk_prb_d1_jaxref_r8_0d6f52'

def setup_inputs(seed: int=0):
    np.random.seed(seed)
    _w = jnp.asarray

    def _L0_attn_setup():
        import jax, jax.numpy as jnp
        import numpy as np
        DIM_IN, DIM_K, DIM_V, N_QUERY = (128, 128, 128, 8)

        def _kaiming_uniform(key, shape):
            fan_in = shape[-2] if len(shape) > 1 else shape[-1]
            gain = 1.0 / np.sqrt(3.0)
            bound = gain * np.sqrt(3.0 / fan_in)
            return jax.random.uniform(key, shape, jnp.float32, -bound, bound)
        key = jax.random.key(seed)
        kx, kq, kk, kv, ko = jax.random.split(key, 5)
        x = jax.random.normal(kx, (4, 256, DIM_IN), dtype=jnp.float32)
        proj_q = _kaiming_uniform(kq, (N_QUERY, DIM_IN, DIM_K))
        proj_k = _kaiming_uniform(kk, (DIM_IN, DIM_K))
        proj_v = _kaiming_uniform(kv, (DIM_IN, DIM_V))
        proj_o = _kaiming_uniform(ko, (N_QUERY, DIM_IN, DIM_V))
        return {'x': x, 'proj_q': proj_q, 'proj_k': proj_k, 'proj_v': proj_v, 'proj_o': proj_o}
    _L0_attn_in = _L0_attn_setup()

    def _L0_ffn_setup():
        import jax, jax.numpy as jnp
        import numpy as np
        A, M, H = (4, 128, 128)
        E, N = (8, 512)
        key = jax.random.key(seed)
        kx, k1, k2 = jax.random.split(key, 3)
        x = jax.random.normal(kx, (A, M, H), dtype=jnp.float32)
        w1 = jax.random.normal(k1, (E, H, N), dtype=jnp.float32) * 0.02
        w2 = jax.random.normal(k2, (E, N, H), dtype=jnp.float32) * 0.02
        return {'x': x, 'w1': w1, 'w2': w2}
    _L0_ffn_in = _L0_ffn_setup()
    _d = {'L0_attn_x': _L0_attn_in['x'], 'L0_attn_proj_q': _L0_attn_in['proj_q'], 'L0_attn_proj_k': _L0_attn_in['proj_k'], 'L0_attn_proj_v': _L0_attn_in['proj_v'], 'L0_attn_proj_o': _L0_attn_in['proj_o'], 'L0_ffn_w1': _L0_ffn_in['w1'], 'L0_ffn_w2': _L0_ffn_in['w2']}
    _x0 = _d['L0_attn_x']
    _d['L0_attn_x'] = jax.random.normal(jax.random.fold_in(jax.random.key(seed), 1), (8, 1024, 128), dtype=_x0.dtype)
    del _x0
    return _d

def reference(L0_attn_x, L0_attn_proj_q, L0_attn_proj_k, L0_attn_proj_v, L0_attn_proj_o, L0_ffn_w1, L0_ffn_w2):

    def _L0_attn_ref(x, proj_q, proj_k, proj_v, proj_o):
        import jax, jax.numpy as jnp
        import numpy as np
        DIM_IN, DIM_K, DIM_V, N_QUERY = (128, 128, 128, 8)

        def _kaiming_uniform(key, shape):
            fan_in = shape[-2] if len(shape) > 1 else shape[-1]
            gain = 1.0 / np.sqrt(3.0)
            bound = gain * np.sqrt(3.0 / fan_in)
            return jax.random.uniform(key, shape, jnp.float32, -bound, bound)
        Q = jnp.einsum('bnd,hdk->bhnk', x, proj_q)
        K = jnp.einsum('bmd,dk->bmk', x, proj_k)
        V = jnp.einsum('bmd,dv->bmv', x, proj_v)
        logits = jnp.einsum('bhnk,bmk->bhnm', Q, K)
        weights = jax.nn.softmax(logits, axis=-1)
        O = jnp.einsum('bhnm,bmv->bhnv', weights, V)
        Y = jnp.einsum('bhnv,hdv->bnd', O, proj_o)
        return Y

    def _L0_ffn_ref(x, w1, w2):
        import jax, jax.numpy as jnp
        import numpy as np
        A, M, H = (4, 128, 128)
        E, N = (8, 512)
        mid = jnp.einsum('amh,ehn->aemn', x, w1)
        out = jnp.einsum('aemn,enh->amh', mid, w2)
        return out
    x = L0_attn_x
    xn = _layernorm(x, axis=-1)
    x = x + _L0_attn_ref(xn, L0_attn_proj_q, L0_attn_proj_k, L0_attn_proj_v, L0_attn_proj_o) + _L0_ffn_ref(xn, L0_ffn_w1, L0_ffn_w2)
    return x

_drawn_inputs = setup_inputs


def setup_inputs(seed=0):
    import zlib

    import numpy as np

    out = dict(_drawn_inputs(seed))
    spreads = {}
    factors = {}
    for name, (base, spread) in spreads.items():
        noise = np.random.default_rng([zlib.crc32(name.encode()), seed]).standard_normal(out[name].shape)
        drawn = base * np.exp(spread * noise) if base else spread * noise
        out[name] = jnp.asarray(drawn.astype(out[name].dtype))
    for name, factor in factors.items():
        out[name] = (out[name] * factor).astype(out[name].dtype)
    return out
```

```python
import math

import concourse.bass as bass
from concourse import mybir
from contextlib import ExitStack

F32, F16, U32 = mybir.dt.float32, mybir.dt.float16, mybir.dt.uint32
ALU = mybir.AluOpType
ACT = mybir.ActivationFunctionType
AX_X = mybir.AxisListType.X

P = 128
EPS = 1e-5
TINY = 2.0 ** -100
EXPONENT = 0x7F800000
LOG_BOOST = math.log(16.0)


def attention_ffn(nc, x, wq, wk, wv, wo, w1, w2, out):
    B, N, D = x.shape
    H = wq.shape[0]
    E, _, M = w1.shape
    assert D == P and N % 1024 == 0 and H == 8
    NT = N // P
    TILES = B * NT
    PAIRS = B * H
    UNITS = 2 * PAIRS
    HALF = N // 2
    HT = NT // 2
    STEPS = NT // 2
    MC = M // P
    YW = P + 2
    RING = 4
    AHEAD = NT + 1
    LN_END = TILES - AHEAD
    SEGMENTS = [
        (0, 1, True, False, True, True, True),
        (1, H, True, False, True, True, True),
        (H, LN_END, True, True, True, True, True),
        (LN_END, PAIRS - 2, False, True, True, True, True),
        (PAIRS - 2, PAIRS - 1, False, True, True, False, True),
        (PAIRS - 1, PAIRS, False, True, False, False, False),
    ]
    FFN_AT = 1

    x_tiles = x.rearrange("b (t p) d -> p (b t) d", p=P)
    out_tiles = out.rearrange("b (t p) d -> p (b t) d", p=P)

    ctx = ExitStack()
    with ctx:
        def sb(name, shape, dt):
            return ctx.enter_context(nc.sbuf_tensor(name, shape, dt))

        def pb(name, shape, dt=F32):
            return ctx.enter_context(nc.psum_tensor(name, shape, dt))

        def sem(name):
            return ctx.enter_context(nc.semaphore(name))

        xacc = sb("xacc", [P, TILES, D], F32)
        xn_hi = sb("xn_hi", [P, TILES, D], F16)
        xn_lo = sb("xn_lo", [P, TILES, D], F16)
        xT = sb("xT", [P, 2, TILES * P], F16)
        xn32 = sb("xn32", [P, D], F32)
        stats = sb("stats", [P, 6], F32)
        mean_var = sb("mean_var", [P, AHEAD + 1, 2], F32)
        var_eps = sb("var_eps", [P, AHEAD + 1], F32)
        rstd = sb("rstd", [P, AHEAD + 1], F32)
        minus_half = sb("minus_half", [P, AHEAD], F32)
        a_hi = sb("a_hi", [P, H, P], F16)
        a_lo = sb("a_lo", [P, H, P], F16)
        c_hi = sb("c_hi", [P, H, YW], F16)
        c_lo = sb("c_lo", [P, H, YW], F16)
        f32w = sb("f32w", [P, D], F32)
        f_hi = sb("f_hi", [P, D], F16)
        f_lo = sb("f_lo", [P, D], F16)
        amax = sb("amax", [P, 3], F32)
        amax_all = sb("amax_all", [P, 3], F32)
        amax_floor = sb("amax_floor", [P, 3], F32)
        scale = sb("scale", [P, 3], F32)
        inv_scale = sb("inv_scale", [P, 3], F32)
        ident = sb("ident", [P, P], F32)
        ident16 = sb("ident16", [P, P], F16)
        centre = sb("centre", [P, P], F32)
        g_hi = sb("g_hi", [P, RING * HALF], F16)
        g_lo = sb("g_lo", [P, RING * HALF], F16)
        row_max = sb("row_max", [P, 2, HT], F16)
        minus_max = sb("minus_max", [HT, 2, P], F16)
        pr32 = sb("pr32", [P, RING, 2 * HALF], F32)
        pr_hi = sb("pr_hi", [P, RING, 2 * HALF], F16)
        pr_lo = sb("pr_lo", [P, RING, 2 * HALF], F16)
        t_hi = sb("t_hi", [P, HALF], F16)
        t_lo = sb("t_lo", [P, HALF], F16)
        recip = sb("recip", [P, 2], F32)
        recip_c = sb("recip_c", [P, 2], F32)
        w1_e = sb("w1_e", [P, 2, M], F32)
        w2_e = sb("w2_e", [P, 2, MC, D], F32)
        wq_sb = pr32[:, 0, :].rearrange("p (h k) -> p h k", h=H)
        wo_sb = pr32[:, 1, :].rearrange("p (h k) -> p h k", h=H)
        wqT = pr32[:, 2, :].rearrange("p (h k) -> p h k", h=H)
        woT = pr32[:, 3, :]
        wkv = sb("wkv", [P, 2, P], F32)
        wkvT = sb("wkvT", [P, 2 * P], F32)
        w1T = sb("w1T", [P, 2, M], F32)
        boost = sb("boost", [P, 1], F32)

        scores = [pb(f"scores{n}", [P, 2 * HALF]) for n in range(2)]
        max_ps = pb("max_ps", [P, 2 * HALF])
        t_ps = pb("t_ps", [P, HALF])
        misc = pb("misc", [P, 512])
        misc16 = misc[:, :].bitcast(F16)
        max16 = max_ps[:, :].bitcast(F16)

        w_in, kv_in, x_in, x_in2 = sem("w_in"), sem("kv_in"), sem("x_in"), sem("x_in2")
        w1_in = [sem("w1_in0"), sem("w1_in1")]
        consts, slot_set = sem("consts"), sem("slot_set")
        transposed, evacuated, folded = sem("transposed"), sem("evacuated"), sem("folded")
        amax_ready, amax_spread, scales_a, scales, hi_ready, weights_ready = (
            sem(n) for n in ("amax_ready", "amax_spread", "scales_a", "scales", "hi_ready", "weights_ready"))
        ln_stats, ln_mean, ln_var, ln_rstd, ln_xn32, ln_hi, xn_ready = (
            sem(n) for n in ("ln_stats", "ln_mean", "ln_var", "ln_rstd", "ln_xn32", "ln_hi", "xn_ready"))
        xT_ps, xT_ready = sem("xT_ps"), sem("xT_ready")
        g_ps, g_hi_ready, g_lo_ready = sem("g_ps"), sem("g_hi_ready"), sem("g_lo_ready")
        max_scores, max_done = sem("max_scores"), sem("max_done")
        max_turned, max_negated, max_landed = sem("max_turned"), sem("max_negated"), sem("max_landed")
        scores_ready, exp_done, p_hi_ready, p_lo_ready = (
            sem(n) for n in ("scores_ready", "exp_done", "p_hi_ready", "p_lo_ready"))
        pv_done, t_hi_ready, t_lo_ready = sem("pv_done"), sem("t_hi_ready"), sem("t_lo_ready")
        y_ps, y_recip, y_recip_c, y_added = sem("y_ps"), sem("y_recip"), sem("y_recip_c"), sem("y_added")
        ffn_ps, tile_done = sem("ffn_ps"), sem("tile_done")
        w1_turned, w1_evacuated, f_ps, f_copied = (
            sem(n) for n in ("w1_turned", "w1_evacuated", "f_ps", "f_copied"))
        stored = sem("stored")

        block = ctx.enter_context(nc.Block())

        def x_hi(tile, count=1):
            return xT[:, 0, bass.ds(tile * P, count * P)]

        def x_lo(tile, count=1):
            return xT[:, 1, bass.ds(tile * P, count * P)]

        def g_slot(tensor, pair, half, at=0, width=HALF):
            return tensor[:, bass.ds((pair % 2) * (2 * HALF) + (half * HALF + at), width)]

        @block.sync
        def _(sp):
            sp.dma_start(xacc[:, 0:NT, :], x_tiles[:, 0:NT, :]).then_inc(x_in, 16)
            sp.dma_start(wkv[:, 0, :], wk).then_inc(kv_in, 16)
            sp.dma_start(wkv[:, 1, :], wv).then_inc(kv_in, 16)
            sp.dma_start(wo_sb, wo.rearrange("h d v -> d h v")).then_inc(w_in, 16)
            sp.dma_start(xacc[:, NT:TILES, :], x_tiles[:, NT:TILES, :]).then_inc(x_in2, 16)

            def load_expert(e):
                sp.dma_start(w1_e[:, e % 2, :], w1[e]).then_inc(w1_in[e % 2], 16)
                sp.dma_start(w2_e[:, e % 2, :, :], w2[e].rearrange("(c p) d -> p c d", p=P))\
                  .then_inc(w1_in[e % 2], 16)

            for e in range(2):
                load_expert(e)

            def ring_at(pair, half):
                return (pair % 2) * (2 * HALF) + half * HALF

            def early(value):
                return value if isinstance(value, int) else sp.snap(value)

            def put_max(at, half, negated):
                sp.wait_ge(max_negated, negated)
                row = g_hi[0:1, bass.ds(at, HALF)]
                sp.dma_start(row.rearrange("a (t c) -> a t c", c=P), minus_max[:, half, :])\
                  .then_inc(max_landed, 16)

            put_max(0, 0, 1)

            def pair(p, ln, finish, g0, g1, maxima):
                odd_at, even_at = early(ring_at(p, 1)), early(ring_at(p + 1, 0))
                odd_negated, even_negated = early(2 * p + 2), early(2 * p + 3)
                if finish:
                    tile, done = early(p - H), early(p - (H - 1))
                    sp.wait_ge(tile_done, done)
                    sp.dma_start(out_tiles[:, bass.ds(tile, 1), :], xacc[:, bass.ds(tile, 1), :])\
                      .then_inc(stored, 16)
                put_max(odd_at, 1, odd_negated)
                if maxima:
                    put_max(even_at, 0, even_negated)

            for n, (first, last, *does) in enumerate(SEGMENTS):
                if last - first == 1:
                    pair(first, *does)
                else:
                    with sp.Fori(first, last) as p:
                        pair(p, *does)
                if n == FFN_AT:
                    for e in range(2, E):
                        sp.wait_ge(f_ps, e - 1)
                        load_expert(e)
            sp.wait_ge(tile_done, PAIRS - H + 1)
            sp.dma_start(out_tiles[:, TILES - NT:TILES - HT, :], xacc[:, TILES - NT:TILES - HT, :])\
              .then_inc(stored, 16)
            sp.wait_ge(y_added, 2 * UNITS)
            sp.dma_start(out_tiles[:, TILES - HT:TILES, :], xacc[:, TILES - HT:TILES, :])\
              .then_inc(stored, 16)
            sp.wait_ge(stored, 16 * (PAIRS - H + 2))

        @block.gpsimd
        def _(pool):
            pool.memset(ident[:, :], 0.0).then_inc(consts, 1)
            pool.memset(minus_half[:, :], -0.5).then_inc(consts, 1)
            pool.wait_ge(consts, 1)
            pool.affine_select(out=ident[:, :], in_=ident[:, :], compare_op=ALU.not_equal, fill=1.0,
                               base=0, pattern=[[-1, P]], channel_multiplier=1).then_inc(consts, 1)
            pool.wait_ge(consts, 3)
            pool.tensor_copy(centre[:, :], ident[:, :]).then_inc(consts, 1)
            pool.tensor_copy(ident16[:, :], ident[:, :]).then_inc(consts, 1)
            pool.wait_ge(consts, 5)
            pool.memset(centre[0:1, :], -1.0).then_inc(consts, 1)
            pool.wait_ge(consts, 6)
            pool.memset(centre[0:1, 0:1], 0.0).then_inc(consts, 1)
            pool.wait_ge(ln_var, 1)
            pool.tensor_tensor(rstd[:, 0:AHEAD], var_eps[:, 0:AHEAD], minus_half[:, :], ALU.pow)\
                .then_inc(ln_rstd, AHEAD)
            pool.wait_ge(amax_ready, 2)
            pool.partition_all_reduce(amax_all[:, 0:2], amax[:, 0:2], P, bass.bass_isa.ReduceOp.max)\
                .then_inc(amax_spread, 1)

            def pair(p, ln, finish, g0, g1, maxima):
                for half in range(2):
                    for s in range(STEPS):
                        i = 2 * STEPS * p + STEPS * half + s
                        if ln and half == 0 and s == 3:
                            pool.wait_ge(ln_var, p + 2)
                            pool.tensor_tensor(rstd[:, AHEAD:AHEAD + 1], var_eps[:, AHEAD:AHEAD + 1],
                                               minus_half[:, 0:1], ALU.pow).then_inc(ln_rstd, 1)
                        pool.wait_ge(p_hi_ready, i + 1)
                        if not isinstance(i, int) or i >= RING:
                            pool.wait_ge(pv_done, i - (RING - 1))
                        pool.tensor_tensor(pr_lo[:, s % RING, :], pr32[:, s % RING, :],
                                           pr_hi[:, s % RING, :], ALU.subtract).then_inc(p_lo_ready, 1)

            for n, (first, last, *does) in enumerate(SEGMENTS):
                if last - first == 1:
                    pair(first, *does)
                else:
                    with pool.Fori(first, last) as p:
                        pair(p, *does)
                if n == FFN_AT:
                    pool.wait_ge(amax_ready, 3)
                    pool.partition_all_reduce(amax_all[:, 2:3], amax[:, 2:3], P,
                                              bass.bass_isa.ReduceOp.max).then_inc(amax_spread, 1)

        @block.scalar
        def _(act):
            act.dma_start(wq_sb, wq.rearrange("h d k -> d h k")).then_inc(w_in, 16)
            act.wait_ge(transposed, 1)
            act.activation(wqT, scores[0][:, :].rearrange("p (h k) -> p h k", h=H), ACT.Copy)\
               .then_inc(evacuated, 1)
            act.wait_ge(transposed, 3)
            act.activation(woT, scores[1][:, :], ACT.Copy).then_inc(evacuated, 1)
            act.wait_ge(scales, 1)
            act.activation(a_hi[:, :, :], scores[0][:, :].rearrange("p (h k) -> p h k", h=H), ACT.Copy,
                           scale=inv_scale[:, 0:1]).then_inc(hi_ready, 1)
            act.activation(c_hi[:, :, 0:P], scores[1][:, :].rearrange("p (h k) -> p h k", h=H), ACT.Copy,
                           scale=inv_scale[:, 1:2]).then_inc(hi_ready, 1)

            def g_high(source, pair, half, unit):
                act.wait_ge(g_ps, unit + 1)
                act.activation(g_slot(g_hi, pair, half), source, ACT.Copy).then_inc(g_hi_ready, 1)

            for u, source in enumerate((scores[0][:, 0:HALF], scores[0][:, HALF:2 * HALF], scores[1][:, 0:HALF])):
                g_high(source, u // 2, u % 2, u)

            def t_high(unit):
                act.wait_ge(pv_done, STEPS * (unit + 1))
                if not isinstance(unit, int) or unit > 0:
                    act.wait_ge(y_ps, 2 * unit)
                act.activation(t_hi[:, :], t_ps[:, :], ACT.Copy).then_inc(t_hi_ready, 1)

            def pair(p, ln, finish, g0, g1, maxima):
                start = isinstance(p, int) and p == 0
                for half in range(2):
                    u = 2 * p + half
                    for s in range(STEPS):
                        i = 2 * STEPS * p + STEPS * half + s
                        act.wait_ge(scores_ready, i + 1)
                        if not (start and half == 0):
                            act.wait_ge(p_lo_ready, i - (RING - 1))
                        act.activation(pr32[:, s % RING, :], scores[s % 2][:, :], ACT.Exp,
                                       bias=boost[:, 0:1], scale=scale[:, 0:1]).then_inc(exp_done, 1)
                        if s == 0 and (g0, g1)[half]:
                            g_high(misc[:, :], p + 1 + half, 1 - half, u + 3)
                        if s == 1 and not (start and half == 0):
                            t_high(u - 1)
                        act.wait_ge(exp_done, i + 1)
                        if not (start and half == 0):
                            act.wait_ge(pv_done, i - (RING - 1))
                        act.activation(pr_hi[:, s % RING, :], pr32[:, s % RING, :], ACT.Copy)\
                           .then_inc(p_hi_ready, 1)

            for n, (first, last, *does) in enumerate(SEGMENTS):
                if last - first == 1:
                    pair(first, *does)
                else:
                    with act.Fori(first, last) as p:
                        pair(p, *does)
                if n == FFN_AT:
                    for e in range(E):
                        act.wait_ge(w1_turned, e + 1)
                        if e >= 2:
                            act.wait_ge(f_ps, e - 1)
                        act.activation(w1T[:, e % 2, :], max_ps[:, (e % 2) * 512:(e % 2) * 512 + M], ACT.Copy)\
                           .then_inc(w1_evacuated, 1)
            t_high(UNITS - 1)

        @block.tensor
        def _(pe):
            def three_pass(dst, lhs_hi, lhs_lo, rhs_hi, rhs_lo, start=True, stop=True):
                pe.matmul(dst, lhs_hi, rhs_hi, start=start, stop=False)
                pe.matmul(dst, lhs_hi, rhs_lo, start=False, stop=False)
                return pe.matmul(dst, lhs_lo, rhs_hi, start=False, stop=stop)

            pe.wait_ge(consts, 7)
            pe.wait_ge(w_in, 32)
            pe.wait_ge(kv_in, 32)
            for h in range(H):
                last = pe.matmul(scores[0][:, h * P:(h + 1) * P], wq_sb[:, h, :], centre[:, :], start=True, stop=True)
            last.then_inc(transposed, 1)
            for n in range(2):
                last = pe.matmul(t_ps[:, n * P:(n + 1) * P], wkv[:, n, :], centre[:, :], start=True, stop=True)
            last.then_inc(transposed, 1)
            for h in range(H):
                last = pe.matmul(scores[1][:, h * P:(h + 1) * P], wo_sb[:, h, :], ident[:, :], start=True, stop=True)
            last.then_inc(transposed, 1)

            for t in range(AHEAD):
                pe.wait_ge(xn_ready, t + 1)
                dst = (max16[:, t * 2 * P:(t + 1) * 2 * P] if t < NT else misc16[:, 0:2 * P])
                pe.transpose(dst[:, 0:P], xn_hi[:, t, :], ident16[:, :])
                last = pe.transpose(dst[:, P:2 * P], xn_lo[:, t, :], ident16[:, :])
                if t in (HT - 1, NT - 1, AHEAD - 1):
                    last.then_inc(xT_ps, 1)

            pe.wait_ge(evacuated, 3)
            for h in range(H):
                last = pe.matmul(scores[0][:, h * P:(h + 1) * P], wqT[:, h, :], wkvT[:, 0:P], start=True, stop=True)
            last.then_inc(folded, 1)
            for n in range(2):
                last = pe.matmul(scores[1][:, n * 512:(n + 1) * 512], wkvT[:, P:2 * P],
                                 woT[:, n * 512:(n + 1) * 512], start=True, stop=True)
            last.then_inc(folded, 1)

            def batch_tile(pair):
                return (pair // H) * NT

            def project(dst, pair, half):
                tile = batch_tile(pair) + half * HT
                h = pair % H
                a_h, a_l = a_hi[:, bass.ds(h, 1), :], a_lo[:, bass.ds(h, 1), :]
                three_pass(dst, a_h, a_l, x_hi(tile, HT), x_lo(tile, HT)).then_inc(g_ps, 1)

            def max_tile(dst, pair, half, t):
                queries = g_slot(g_hi, pair, half, t * P, P)
                for n in range(2):
                    last = pe.matmul(dst[:, n * HALF:(n + 1) * HALF], queries,
                                     x_hi(batch_tile(pair) + n * HT, HT), start=True, stop=True)
                last.then_inc(max_scores, 1)

            def turn_max(unit, slot):
                pe.wait_ge(max_done, HT * (unit + 1))
                pe.transpose(misc16[0:HT, 0:P], row_max[:, slot, :], ident16[:, :]).then_inc(max_turned, 1)

            pe.wait_ge(weights_ready, 2)
            pe.wait_ge(xT_ready, AHEAD)
            for u, dst in enumerate((scores[0][:, 0:HALF], scores[0][:, HALF:2 * HALF], scores[1][:, 0:HALF])):
                project(dst, u // 2, u % 2)
            for j in range(2 * HT):
                if j == 0:
                    pe.wait_ge(g_lo_ready, 3)
                if j >= 3:
                    pe.wait_ge(max_done, j - 2)
                max_tile((max_ps, scores[0], scores[1])[j % 3], 0, j // HT, j % HT)
            turn_max(0, 0)

            def weigh(k_pair, k_step, ring):
                tile = batch_tile(k_pair) + 2 * k_step
                for j in range(2):
                    first, last = k_step == 0 and j == 0, k_step == STEPS - 1 and j == 1
                    keys_hi, keys_lo = xn_hi[:, bass.ds(tile + j, 1), :], xn_lo[:, bass.ds(tile + j, 1), :]
                    p_hi, p_lo = pr_hi[:, ring, j * HALF:(j + 1) * HALF], pr_lo[:, ring, j * HALF:(j + 1) * HALF]
                    done = three_pass(t_ps[:, :], keys_hi, keys_lo, p_hi, p_lo, start=first, stop=last)
                done.then_inc(pv_done, 1)

            def head_out(pair, g):
                c_h, c_l = c_hi[:, bass.ds(pair % H, 1), :], c_lo[:, bass.ds(pair % H, 1), :]
                for q in range(2):
                    cols = slice((2 * g + q) * P, (2 * g + q + 1) * P)
                    last = three_pass(misc[:, q * 256:q * 256 + YW], t_hi[:, cols], t_lo[:, cols], c_h, c_l)
                last.then_inc(y_ps, 1)

            def ffn(dst, tile):
                return three_pass(dst, x_hi(tile), x_lo(tile), f_hi[:, :], f_lo[:, :])

            def pair(p, ln, finish, g0, g1, maxima):
                start = isinstance(p, int) and p == 0
                for half in range(2):
                    u = 2 * p + half
                    begun = not (start and half == 0)
                    before = p - 1 + half
                    has_g = (g0, g1)[half]
                    for s in range(STEPS):
                        i = 2 * STEPS * p + STEPS * half + s
                        if s == 0:
                            pe.wait_ge(max_landed, 16 * (u + 1))
                        if begun or s >= 2:
                            pe.wait_ge(exp_done, i - 1)
                        for j in range(2):
                            tile = batch_tile(p) + 2 * s + j
                            last = three_pass(scores[s % 2][:, j * HALF:(j + 1) * HALF], x_hi(tile), x_lo(tile),
                                              g_slot(g_hi, p, half), g_slot(g_lo, p, half))
                        last.then_inc(scores_ready, 1)

                        if s == 0 and has_g:
                            if begun and not (start and half == 1):
                                pe.wait_ge(y_added, 2 * u - 2)
                            else:
                                pe.wait_ge(max_negated, 1)
                            pe.wait_ge(xT_ready, p + AHEAD if ln else TILES)
                            project(misc[:, :], p + 1 + half, 1 - half)
                        if s == 1 and (half == 0 or maxima):
                            if half == 0 and finish:
                                pe.wait_ge(tile_done, p - (H - 1))
                            elif half == 1 and ln:
                                pe.wait_ge(xT_ready, p + AHEAD + 1)
                            elif has_g:
                                pe.wait_ge(g_lo_ready, u + 4)
                            turn_max(u + 1, 1 - half)
                        if s == 3 and begun:
                            pe.wait_ge(y_added, 2 * u - 1)
                            head_out(before, 1)
                        if maxima:
                            if s == 0:
                                pe.wait_ge(g_lo_ready, u + 3)
                            pe.wait_ge(max_done, HT * (u + 2) + s)
                            max_tile(max_ps, p + 1, half, s)

                        if begun or s >= 2:
                            pe.wait_ge(p_lo_ready, i - 1)
                            if s == 2 and begun:
                                pe.wait_ge(t_lo_ready, u)
                            if s < 2:
                                weigh(before, s + 2, (s + 2) % RING)
                            else:
                                weigh(p, s - 2, (s + 2) % RING)

                        if s == 0 and half == 0 and finish:
                            if has_g:
                                pe.wait_ge(g_lo_ready, u + 4)
                            else:
                                pe.wait_ge(y_added, 2 * u - 2)
                            pe.wait_ge(weights_ready, 3)
                            ffn(misc[:, 0:D], p - H).then_inc(ffn_ps, 1)
                        if s == 0 and half == 1 and ln:
                            pe.wait_ge(g_lo_ready, u + 4)
                            pe.wait_ge(xn_ready, p + AHEAD + 1)
                            pe.transpose(misc16[:, 0:P], xn_hi[:, bass.ds(p + AHEAD, 1), :], ident16[:, :])
                            pe.transpose(misc16[:, P:2 * P], xn_lo[:, bass.ds(p + AHEAD, 1), :], ident16[:, :])\
                              .then_inc(xT_ps, 1)
                        if s == 2 and begun:
                            if half == 0 or maxima:
                                pe.wait_ge(max_negated, u + 2)
                            head_out(before, 0)

            def fold_ffn():
                for e in range(E + 1):
                    if e < E:
                        pe.wait_ge(w1_in[e % 2], 32 * (e // 2 + 1))
                        if e == 0:
                            pe.wait_ge(max_done, HT * (2 * H + 2))
                        if e >= 2:
                            pe.wait_ge(w1_evacuated, e - 1)
                        for c in range(MC):
                            at = (e % 2) * 512 + c * P
                            last = pe.matmul(max_ps[:, at:at + P], w1_e[:, e % 2, c * P:(c + 1) * P],
                                             centre[:, :], start=True, stop=True)
                        last.then_inc(w1_turned, 1)
                    if e >= 1:
                        d = e - 1
                        if d == 0:
                            pe.wait_ge(y_added, 4 * H - 2)
                        pe.wait_ge(w1_evacuated, d + 1)
                        for c in range(MC):
                            last = pe.matmul(misc[:, 0:D], w1T[:, d % 2, c * P:(c + 1) * P], w2_e[:, d % 2, c, :],
                                             start=d == 0 and c == 0, stop=d == E - 1 and c == MC - 1)
                        last.then_inc(f_ps, 1)
                pe.wait_ge(f_copied, 1)

            for n, (first, last_pair, *does) in enumerate(SEGMENTS):
                if last_pair - first == 1:
                    pair(first, *does)
                else:
                    with pe.Fori(first, last_pair) as p:
                        pair(p, *does)
                if n == FFN_AT:
                    fold_ffn()

            for k in range(2):
                pe.wait_ge(p_lo_ready, STEPS * UNITS - 1 + k)
                weigh(PAIRS - 1, STEPS - 2 + k, (STEPS - 2 + k) % RING)
            pe.wait_ge(exp_done, STEPS * UNITS)
            for t in range(NT):
                last = ffn(scores[0][:, t * P:(t + 1) * P], TILES - NT + t)
            last.then_inc(ffn_ps, 1)
            pe.wait_ge(t_lo_ready, UNITS)
            pe.wait_ge(y_added, 2 * UNITS - 2)
            head_out(PAIRS - 1, 0)
            pe.wait_ge(y_added, 2 * UNITS - 1)
            head_out(PAIRS - 1, 1)

        @block.vector
        def _(dve):
            dve.memset(xn_hi[:, :, 0:1], 1.0).then_inc(slot_set, 1)
            dve.memset(xn_lo[:, :, 0:1], 0.0).then_inc(slot_set, 1)
            dve.memset(boost[:, :], LOG_BOOST).then_inc(slot_set, 1)
            dve.memset(c_hi[:, :, P:YW], 0.0).then_inc(slot_set, 1)
            dve.memset(c_lo[:, :, P:YW], 0.0).then_inc(slot_set, 1)
            dve.wait_ge(slot_set, 5)
            dve.memset(c_hi[0:1, :, P:P + 1], 1.0).then_inc(slot_set, 1)

            def tile_stats(t, slot, count):
                dve.bn_stats(stats[:, :], xacc[:, bass.ds(t, 1), :]).then_inc(ln_stats, 1)
                if isinstance(t, int):
                    dve.wait_ge(ln_stats, count)
                    tile_mean(slot)

            def tile_mean(slot):
                dve.bn_aggr(mean_var[:, slot, :], stats[:, :]).then_inc(ln_mean, 1)

            def normalise(t, slot, count):
                dve.tensor_scalar(xn32[:, 1:D], xacc[:, bass.ds(t, 1), 1:D], mean_var[:, slot, 0:1],
                                  rstd[:, slot:slot + 1], ALU.subtract, ALU.mult).then_inc(ln_xn32, 1)
                dve.wait_ge(ln_xn32, count)
                dve.tensor_copy(xn_hi[:, bass.ds(t, 1), 1:D], xn32[:, 1:D]).then_inc(ln_hi, 1)
                dve.wait_ge(ln_hi, count)
                dve.tensor_tensor(xn_lo[:, bass.ds(t, 1), 1:D], xn32[:, 1:D], xn_hi[:, bass.ds(t, 1), 1:D],
                                  ALU.subtract).then_inc(xn_ready, 1)

            dve.wait_ge(x_in, 16)
            for t in range(AHEAD):
                if t == NT:
                    dve.wait_ge(x_in2, 16)
                if t > 0:
                    dve.wait_ge(ln_mean, t)
                tile_stats(t, t, t + 1)
            dve.wait_ge(ln_mean, AHEAD)
            dve.tensor_scalar_add(var_eps[:, 0:AHEAD], mean_var[:, 0:AHEAD, 1], EPS).then_inc(ln_var, 1)
            dve.wait_ge(transposed, 2)
            dve.tensor_copy(wkvT[:, :], t_ps[:, 0:2 * P]).then_inc(evacuated, 1)
            dve.wait_ge(ln_rstd, AHEAD)
            for t in range(AHEAD):
                if t > 0:
                    dve.wait_ge(xn_ready, t)
                normalise(t, t, t + 1)

            def power_of_two(n0, n1, done):
                dve.tensor_scalar_max(amax_floor[:, n0:n1], amax_all[:, n0:n1], TINY).then_inc(scales_a, 1)
                dve.wait_ge(scales_a, 2 * done + 1)
                dve.tensor_scalar(scale[:, n0:n1].bitcast(U32), amax_floor[:, n0:n1].bitcast(U32), EXPONENT, None,
                                  ALU.bitwise_and).then_inc(scales_a, 1)
                dve.wait_ge(scales_a, 2 * done + 2)
                dve.reciprocal(inv_scale[:, n0:n1], scale[:, n0:n1]).then_inc(scales, 1)
                dve.wait_ge(scales, done + 1)

            for n in range(2):
                dve.wait_ge(folded, n + 1)
                dve.tensor_reduce(amax[:, n:n + 1], scores[n][:, :], AX_X, ALU.max, apply_absolute_value=True)\
                   .then_inc(amax_ready, 1)
            for n in range(3):
                dve.wait_ge(xT_ps, n + 1)
                if n < 2:
                    src = max16[:, n * 2 * HALF:(n + 1) * 2 * HALF].rearrange("p (t k c) -> p k t c", k=2, c=P)
                    dst = xT[:, :, n * HALF:(n + 1) * HALF].rearrange("p k (t c) -> p k t c", c=P)
                    dve.tensor_copy(dst, src).then_inc(xT_ready, HT)
                else:
                    dve.tensor_copy(xT[:, :, NT * P:(NT + 1) * P], misc16[:, 0:2 * P].rearrange("p (k c) -> p k c", k=2))\
                       .then_inc(xT_ready, 1)
            dve.wait_ge(amax_spread, 1)
            power_of_two(0, 2, 0)
            for n, (hi, lo) in enumerate(((a_hi, a_lo), (c_hi, c_lo))):
                dve.wait_ge(hi_ready, n + 1)
                dve.scalar_tensor_tensor(out=lo[:, :, 0:P], in0=scores[n][:, :].rearrange("p (h k) -> p h k", h=H),
                                         scalar=inv_scale[:, n:n + 1], in1=hi[:, :, 0:P],
                                         op0=ALU.mult, op1=ALU.subtract).then_inc(weights_ready, 1)

            def g_low(source, pair, half, unit):
                dve.wait_ge(g_hi_ready, unit + 1)
                dve.tensor_tensor(g_slot(g_lo, pair, half), source, g_slot(g_hi, pair, half), ALU.subtract)\
                   .then_inc(g_lo_ready, 1)

            def take_max(source, unit, slot, t):
                dve.wait_ge(max_scores, HT * unit + t + 1)
                dve.reduce_max(row_max[:, slot, t:t + 1], source, AX_X).then_inc(max_done, 1)

            def negate_max(unit, slot):
                dve.wait_ge(max_turned, unit + 1)
                if not isinstance(unit, int) or unit >= 2:
                    dve.wait_ge(max_landed, 16 * (unit - 1))
                dve.tensor_scalar_mul(minus_max[:, slot, :], misc16[0:HT, 0:P], -1.0).then_inc(max_negated, 1)

            for u, source in enumerate((scores[0][:, 0:HALF], scores[0][:, HALF:2 * HALF], scores[1][:, 0:HALF])):
                g_low(source, u // 2, u % 2, u)
            for j in range(2 * HT):
                take_max((max_ps, scores[0], scores[1])[j % 3][:, :], j // HT, j // HT, j % HT)
            negate_max(0, 0)

            def add_head(first_tile, g, count):
                dve.wait_ge(y_ps, count + 1)
                if not isinstance(count, int) or count > 0:
                    dve.wait_ge(y_added, count)
                dve.reciprocal(recip[:, :], misc[:, :].rearrange("p (q c) -> p q c", c=256)[:, :, P]).then_inc(y_recip, 1)
                dve.wait_ge(y_recip, count + 1)
                dve.tensor_scalar(recip_c[:, :], recip[:, :], scale[:, 1:2], None, ALU.mult).then_inc(y_recip_c, 1)
                dve.wait_ge(y_recip_c, count + 1)
                for q in range(2):
                    acc = xacc[:, bass.ds(first_tile + (2 * g + q), 1), :]
                    last = dve.scalar_tensor_tensor(out=acc, in0=misc[:, q * 256:q * 256 + D], scalar=recip_c[:, q:q + 1],
                                                    in1=acc, op0=ALU.mult, op1=ALU.add)
                last.then_inc(y_added, 1)

            def pair(p, ln, finish, g0, g1, maxima):
                start = isinstance(p, int) and p == 0
                for half in range(2):
                    u = 2 * p + half
                    begun = not (start and half == 0)
                    before = ((p - 1 + half) // H) * NT + (1 - half) * HT
                    for s in range(STEPS):
                        if s == 1 and (half == 0 or maxima):
                            negate_max(u + 1, 1 - half)
                        if s == 3 and begun:
                            add_head(before, 1, 2 * u - 1)
                        if s == 2 and half == 0 and ln:
                            dve.wait_ge(ln_stats, p + AHEAD + 1)
                        if maxima:
                            take_max(max_ps[:, :], u + 2, half, s)
                        if s == 2 and half == 0 and ln and not start:
                            tile_mean(AHEAD)
                        if s == 0 and (g0, g1)[half]:
                            g_low(misc[:, :], p + 1 + half, 1 - half, u + 3)
                        if s == 0 and half == 0 and finish:
                            dve.wait_ge(ffn_ps, p - (H - 1))
                            dve.wait_ge(y_added, 2 * u - 2)
                            tile = xacc[:, bass.ds(p - H, 1), :]
                            dve.scalar_tensor_tensor(out=tile, in0=misc[:, 0:D], scalar=scale[:, 2:3], in1=tile,
                                                     op0=ALU.mult, op1=ALU.add).then_inc(tile_done, 1)
                        if s == 0 and half == 1 and ln:
                            dve.wait_ge(xT_ps, p + 4)
                            dve.tensor_copy(xT[:, :, bass.ds((p + AHEAD) * P, P)],
                                            misc16[:, 0:2 * P].rearrange("p (k c) -> p k c", k=2)).then_inc(xT_ready, 1)
                        if s == 1 and begun:
                            dve.wait_ge(t_hi_ready, u)
                            dve.tensor_tensor(t_lo[:, :], t_ps[:, :], t_hi[:, :], ALU.subtract).then_inc(t_lo_ready, 1)
                        if s == 1 and half == 0 and ln:
                            dve.wait_ge(ln_mean, p + AHEAD)
                            tile_stats(p + AHEAD, AHEAD, p + AHEAD + 1)
                        if s == 2 and half == 0 and ln:
                            dve.wait_ge(ln_mean, p + AHEAD + 1)
                            dve.tensor_scalar_add(var_eps[:, AHEAD:AHEAD + 1], mean_var[:, AHEAD, 1:2], EPS)\
                               .then_inc(ln_var, 1)
                        if s == 2 and begun:
                            add_head(before, 0, 2 * u - 2)
                        if s == 3 and half == 0 and ln:
                            dve.wait_ge(ln_rstd, p + AHEAD + 1)
                            dve.wait_ge(xn_ready, p + AHEAD)
                            normalise(p + AHEAD, AHEAD, p + AHEAD + 1)

            for n, (first, last_pair, *does) in enumerate(SEGMENTS):
                if last_pair - first == 1:
                    pair(first, *does)
                else:
                    with dve.Fori(first, last_pair) as p:
                        pair(p, *does)
                if n == FFN_AT:
                    dve.wait_ge(f_ps, E)
                    dve.tensor_copy(f32w[:, :], misc[:, 0:D]).then_inc(f_copied, 1)
                    dve.wait_ge(f_copied, 1)
                    dve.tensor_reduce(amax[:, 2:3], f32w[:, :], AX_X, ALU.max, apply_absolute_value=True)\
                       .then_inc(amax_ready, 1)
                    dve.wait_ge(amax_spread, 2)
                    power_of_two(2, 3, 1)
                    dve.tensor_scalar(f_hi[:, :], f32w[:, :], inv_scale[:, 2:3], None, ALU.mult).then_inc(hi_ready, 1)
                    dve.wait_ge(hi_ready, 3)
                    dve.scalar_tensor_tensor(out=f_lo[:, :], in0=f32w[:, :], scalar=inv_scale[:, 2:3], in1=f_hi[:, :],
                                             op0=ALU.mult, op1=ALU.subtract).then_inc(weights_ready, 1)

            dve.wait_ge(t_hi_ready, UNITS)
            dve.tensor_tensor(t_lo[:, :], t_ps[:, :], t_hi[:, :], ALU.subtract).then_inc(t_lo_ready, 1)
            dve.wait_ge(ffn_ps, PAIRS - H + 1)
            dve.wait_ge(y_added, 2 * UNITS - 2)
            tiles = xacc[:, TILES - NT:TILES, :]
            dve.scalar_tensor_tensor(out=tiles, in0=scores[0][:, :].rearrange("p (t d) -> p t d", d=D),
                                     scalar=scale[:, 2:3], in1=tiles, op0=ALU.mult, op1=ALU.add).then_inc(tile_done, 1)
            dve.wait_ge(tile_done, PAIRS - H + 1)
            for g in range(2):
                add_head(TILES - HT, g, 2 * UNITS - 2 + g)


_INS = ['L0_attn_x', 'L0_attn_proj_q', 'L0_attn_proj_k', 'L0_attn_proj_v', 'L0_attn_proj_o', 'L0_ffn_w1', 'L0_ffn_w2']


def kernel(**inputs):
    import numpy as _np
    import concourse.bacc as _bacc
    from concourse import mybir as _mybir
    from concourse.bass_utils import run_bass_kernel_spmd as _run

    nc = _bacc.Bacc("TRN2", target_bir_lowering=False, num_devices=1)
    arrays, args = {}, []
    for name in _INS:
        a = _np.ascontiguousarray(inputs[name])
        arrays[f"in_{name}_dram"] = a
        args.append(nc.dram_tensor(f"in_{name}_dram", a.shape, _mybir.dt.from_np(a.dtype), kind="ExternalInput").ap())
    shape = inputs['L0_attn_x'].shape
    args.append(nc.dram_tensor("out_0_dram", shape, _mybir.dt.float32, kind="ExternalOutput").ap())
    attention_ffn(nc, *args)
    r = _run(nc, [arrays], core_ids=[0])
    return r.results[0]["out_0_dram"]
```

```python
import math

import concourse.bass as bass
from concourse import mybir
from contextlib import ExitStack

F32, F16, U32 = mybir.dt.float32, mybir.dt.float16, mybir.dt.uint32
ALU = mybir.AluOpType
ACT = mybir.ActivationFunctionType
AX_X = mybir.AxisListType.X

P = 128
EPS = 1e-5
TINY = 2.0 ** -100
EXPONENT = 0x7F800000
LOG_BOOST = math.log(16.0)


def attention_ffn(nc, x, wq, wk, wv, wo, w1, w2, out):
    B, N, D = x.shape
    H = wq.shape[0]
    E, _, M = w1.shape
    assert D == P and N % 1024 == 0 and H == 8
    NT = N // P
    TILES = B * NT
    PAIRS = B * H
    UNITS = 2 * PAIRS
    HALF = N // 2
    HT = NT // 2
    STEPS = NT // 2
    MC = M // P
    YW = P + 2
    RING = 4
    AHEAD = NT + 1
    LN_END = TILES - AHEAD
    SEGMENTS = [
        (0, 1, True, False, True, True, True),
        (1, H, True, False, True, True, True),
        (H, LN_END, True, True, True, True, True),
        (LN_END, PAIRS - 2, False, True, True, True, True),
        (PAIRS - 2, PAIRS - 1, False, True, True, False, True),
        (PAIRS - 1, PAIRS, False, True, False, False, False),
    ]
    FFN_AT = 1

    x_tiles = x.rearrange("b (t p) d -> p (b t) d", p=P)
    out_tiles = out.rearrange("b (t p) d -> p (b t) d", p=P)

    ctx = ExitStack()
    with ctx:
        def sb(name, shape, dt):
            return ctx.enter_context(nc.sbuf_tensor(name, shape, dt))

        def pb(name, shape, dt=F32):
            return ctx.enter_context(nc.psum_tensor(name, shape, dt))

        def sem(name):
            return ctx.enter_context(nc.semaphore(name))

        xacc = sb("xacc", [P, TILES, D], F32)
        xn_hi = sb("xn_hi", [P, TILES, D], F16)
        xn_lo = sb("xn_lo", [P, TILES, D], F16)
        xT = sb("xT", [P, 2, TILES * P], F16)
        xn32 = sb("xn32", [P, AHEAD, D], F32)
        stats = sb("stats", [P, AHEAD + 1, 6], F32)
        mean_var = sb("mean_var", [P, AHEAD + 1, 2], F32)
        var_eps = sb("var_eps", [P, AHEAD + 1], F32)
        rstd = sb("rstd", [P, AHEAD + 1], F32)
        minus_half = sb("minus_half", [P, AHEAD], F32)
        a_hi = sb("a_hi", [P, H, P], F16)
        a_lo = sb("a_lo", [P, H, P], F16)
        c_hi = sb("c_hi", [P, H, YW], F16)
        c_lo = sb("c_lo", [P, H, YW], F16)
        f32w = sb("f32w", [P, D], F32)
        f_hi = sb("f_hi", [P, D], F16)
        f_lo = sb("f_lo", [P, D], F16)
        amax = sb("amax", [P, 3], F32)
        amax_all = sb("amax_all", [P, 3], F32)
        amax_floor = sb("amax_floor", [P, 3], F32)
        scale = sb("scale", [P, 3], F32)
        inv_scale = sb("inv_scale", [P, 3], F32)
        ident = sb("ident", [P, P], F32)
        ident16 = sb("ident16", [P, P], F16)
        centre = sb("centre", [P, P], F32)
        g_hi = sb("g_hi", [P, RING * HALF], F16)
        g_lo = sb("g_lo", [P, RING * HALF], F16)
        row_max = sb("row_max", [P, 2, HT], F16)
        minus_max = sb("minus_max", [HT, 2, P], F16)
        pr32 = sb("pr32", [P, RING, 2 * HALF], F32)
        pr_hi = sb("pr_hi", [P, RING, 2 * HALF], F16)
        pr_lo = sb("pr_lo", [P, RING, 2 * HALF], F16)
        t_hi = sb("t_hi", [P, HALF], F16)
        t_lo = sb("t_lo", [P, HALF], F16)
        recip = sb("recip", [P, 2], F32)
        recip_c = sb("recip_c", [P, 2], F32)
        w1_sb = sb("w1_sb", [P, E, M], F32)
        w2_sb = sb("w2_sb", [P, E, MC, D], F32)
        wq_sb = pr32[:, 0, :].rearrange("p (h k) -> p h k", h=H)
        wo_sb = pr32[:, 1, :].rearrange("p (h k) -> p h k", h=H)
        wqT = pr32[:, 2, :].rearrange("p (h k) -> p h k", h=H)
        woT = pr32[:, 3, :]
        wkv = sb("wkv", [P, 2, P], F32)
        wkvT = sb("wkvT", [P, 2 * P], F32)
        w1T = sb("w1T", [P, 2, M], F32)
        boost = sb("boost", [P, 1], F32)

        scores = [pb(f"scores{n}", [P, 2 * HALF]) for n in range(2)]
        max_ps = pb("max_ps", [P, 2 * HALF])
        t_ps = pb("t_ps", [P, HALF])
        misc = pb("misc", [P, 512])
        misc16 = misc[:, :].bitcast(F16)
        max16 = max_ps[:, :].bitcast(F16)

        q_in, o_in, kv_in = sem("q_in"), sem("o_in"), sem("kv_in")
        x_in, x_in2 = sem("x_in"), sem("x_in2")
        ffn_in = sem("ffn_in")
        consts, slot_set = sem("consts"), sem("slot_set")
        transposed, evacuated, kv_ready, folded = (
            sem(n) for n in ("transposed", "evacuated", "kv_ready", "folded"))
        amax_ready, amax_spread, scales_a, scales, hi_ready, weights_ready = (
            sem(n) for n in ("amax_ready", "amax_spread", "scales_a", "scales", "hi_ready", "weights_ready"))
        ln_stats, ln_mean, ln_var, ln_rstd, ln_xn32, ln_hi, xn_ready = (
            sem(n) for n in ("ln_stats", "ln_mean", "ln_var", "ln_rstd", "ln_xn32", "ln_hi", "xn_ready"))
        xT_ps, xT_ready = sem("xT_ps"), sem("xT_ready")
        g_ps, g_hi_ready, g_lo_ready = sem("g_ps"), sem("g_hi_ready"), sem("g_lo_ready")
        max_scores, max_done = sem("max_scores"), sem("max_done")
        max_turned, max_negated, max_landed = sem("max_turned"), sem("max_negated"), sem("max_landed")
        scores_ready, exp_done, p_hi_ready, p_lo_ready = (
            sem(n) for n in ("scores_ready", "exp_done", "p_hi_ready", "p_lo_ready"))
        pv_done, t_hi_ready, t_lo_ready = sem("pv_done"), sem("t_hi_ready"), sem("t_lo_ready")
        y_ps, y_recip, y_recip_c, y_added = sem("y_ps"), sem("y_recip"), sem("y_recip_c"), sem("y_added")
        ffn_ps, tile_done = sem("ffn_ps"), sem("tile_done")
        w1_turned, w1_evacuated, f_ps, f_copied = (
            sem(n) for n in ("w1_turned", "w1_evacuated", "f_ps", "f_copied"))
        stored = sem("stored")

        block = ctx.enter_context(nc.Block())

        def x_hi(tile, count=1):
            return xT[:, 0, bass.ds(tile * P, count * P)]

        def x_lo(tile, count=1):
            return xT[:, 1, bass.ds(tile * P, count * P)]

        def g_slot(tensor, pair, half, at=0, width=HALF):
            return tensor[:, bass.ds((pair % 2) * (2 * HALF) + (half * HALF + at), width)]

        @block.sync
        def _(sp):
            sp.dma_start(wkv[:, 0, :], wk).then_inc(kv_in, 16)
            sp.dma_start(wkv[:, 1, :], wv).then_inc(kv_in, 16)
            sp.dma_start(xacc[:, 0:AHEAD, :], x_tiles[:, 0:AHEAD, :]).then_inc(x_in, 16)
            sp.dma_start(xacc[:, AHEAD:TILES, :], x_tiles[:, AHEAD:TILES, :]).then_inc(x_in2, 16)

            sp.dma_start(w1_sb[:, :, :], w1.rearrange("e h n -> h e n")).then_inc(ffn_in, 16)
            sp.dma_start(w2_sb[:, :, :, :], w2.rearrange("e (c p) d -> p e c d", p=P)).then_inc(ffn_in, 16)

            def ring_at(pair, half):
                return (pair % 2) * (2 * HALF) + half * HALF

            def early(value):
                return value if isinstance(value, int) else sp.snap(value)

            def put_max(at, half, negated):
                sp.wait_ge(max_negated, negated)
                row = g_hi[0:1, bass.ds(at, HALF)]
                sp.dma_start(row.rearrange("a (t c) -> a t c", c=P), minus_max[:, half, :])\
                  .then_inc(max_landed, 16)

            put_max(0, 0, 1)

            def pair(p, ln, finish, g0, g1, maxima):
                odd_at, even_at = early(ring_at(p, 1)), early(ring_at(p + 1, 0))
                odd_negated, even_negated = early(2 * p + 2), early(2 * p + 3)
                if finish:
                    tile, done = early(p - H), early(p - (H - 1))
                    sp.wait_ge(tile_done, done)
                    sp.dma_start(out_tiles[:, bass.ds(tile, 1), :], xacc[:, bass.ds(tile, 1), :])\
                      .then_inc(stored, 16)
                put_max(odd_at, 1, odd_negated)
                if maxima:
                    put_max(even_at, 0, even_negated)

            for n, (first, last, *does) in enumerate(SEGMENTS):
                if last - first == 1:
                    pair(first, *does)
                else:
                    with sp.Fori(first, last) as p:
                        pair(p, *does)
            sp.wait_ge(tile_done, PAIRS - H + 1)
            sp.dma_start(out_tiles[:, TILES - NT:TILES - HT, :], xacc[:, TILES - NT:TILES - HT, :])\
              .then_inc(stored, 16)
            sp.wait_ge(y_added, 2 * UNITS)
            sp.dma_start(out_tiles[:, TILES - HT:TILES, :], xacc[:, TILES - HT:TILES, :])\
              .then_inc(stored, 16)
            sp.wait_ge(stored, 16 * (PAIRS - H + 2))

        @block.gpsimd
        def _(pool):
            pool.memset(ident[:, :], 0.0).then_inc(consts, 1)
            pool.memset(minus_half[:, :], -0.5).then_inc(consts, 1)
            pool.wait_ge(consts, 1)
            pool.affine_select(out=ident[:, :], in_=ident[:, :], compare_op=ALU.not_equal, fill=1.0,
                               base=0, pattern=[[-1, P]], channel_multiplier=1).then_inc(consts, 1)
            pool.wait_ge(consts, 3)
            pool.tensor_copy(centre[:, :], ident[:, :]).then_inc(consts, 1)
            pool.tensor_copy(ident16[:, :], ident[:, :]).then_inc(consts, 1)
            pool.wait_ge(consts, 5)
            pool.memset(centre[0:1, :], -1.0).then_inc(consts, 1)
            pool.wait_ge(consts, 6)
            pool.memset(centre[0:1, 0:1], 0.0).then_inc(consts, 1)
            pool.wait_ge(ln_var, 1)
            pool.tensor_tensor(rstd[:, 0:AHEAD], var_eps[:, 0:AHEAD], minus_half[:, :], ALU.pow)\
                .then_inc(ln_rstd, AHEAD)
            pool.wait_ge(amax_ready, 2)
            pool.partition_all_reduce(amax_all[:, 0:2], amax[:, 0:2], P, bass.bass_isa.ReduceOp.max)\
                .then_inc(amax_spread, 1)

            def pair(p, ln, finish, g0, g1, maxima):
                for half in range(2):
                    for s in range(STEPS):
                        i = 2 * STEPS * p + STEPS * half + s
                        if ln and half == 0 and s == 3:
                            pool.wait_ge(ln_var, p + 2)
                            pool.tensor_tensor(rstd[:, AHEAD:AHEAD + 1], var_eps[:, AHEAD:AHEAD + 1],
                                               minus_half[:, 0:1], ALU.pow).then_inc(ln_rstd, 1)
                        pool.wait_ge(p_hi_ready, i + 1)
                        if not isinstance(i, int) or i >= RING:
                            pool.wait_ge(pv_done, i - (RING - 1))
                        pool.tensor_tensor(pr_lo[:, s % RING, :], pr32[:, s % RING, :],
                                           pr_hi[:, s % RING, :], ALU.subtract).then_inc(p_lo_ready, 1)

            for n, (first, last, *does) in enumerate(SEGMENTS):
                if last - first == 1:
                    pair(first, *does)
                else:
                    with pool.Fori(first, last) as p:
                        pair(p, *does)
                if n == FFN_AT:
                    pool.wait_ge(amax_ready, 3)
                    pool.partition_all_reduce(amax_all[:, 2:3], amax[:, 2:3], P,
                                              bass.bass_isa.ReduceOp.max).then_inc(amax_spread, 1)

        @block.scalar
        def _(act):
            act.dma_start(wq_sb, wq.rearrange("h d k -> d h k")).then_inc(q_in, 16)
            act.dma_start(wo_sb, wo.rearrange("h d v -> d h v")).then_inc(o_in, 16)
            act.wait_ge(transposed, 2)
            act.activation(wqT, scores[0][:, :].rearrange("p (h k) -> p h k", h=H), ACT.Copy)\
               .then_inc(evacuated, 1)
            act.wait_ge(transposed, 3)
            act.activation(woT, scores[1][:, :], ACT.Copy).then_inc(evacuated, 1)
            act.wait_ge(scales, 1)
            act.activation(a_hi[:, :, :], scores[0][:, :].rearrange("p (h k) -> p h k", h=H), ACT.Copy,
                           scale=inv_scale[:, 0:1]).then_inc(hi_ready, 1)
            act.activation(c_hi[:, :, 0:P], scores[1][:, :].rearrange("p (h k) -> p h k", h=H), ACT.Copy,
                           scale=inv_scale[:, 1:2]).then_inc(hi_ready, 1)

            def g_high(source, pair, half, unit):
                act.wait_ge(g_ps, unit + 1)
                act.activation(g_slot(g_hi, pair, half), source, ACT.Copy).then_inc(g_hi_ready, 1)

            for u, source in enumerate((scores[0][:, 0:HALF], scores[0][:, HALF:2 * HALF], t_ps[:, :])):
                g_high(source, u // 2, u % 2, u)

            def t_high(unit):
                act.wait_ge(pv_done, STEPS * (unit + 1))
                if not isinstance(unit, int) or unit > 0:
                    act.wait_ge(y_ps, 2 * unit)
                act.activation(t_hi[:, :], t_ps[:, :], ACT.Copy).then_inc(t_hi_ready, 1)

            def pair(p, ln, finish, g0, g1, maxima):
                start = isinstance(p, int) and p == 0
                for half in range(2):
                    u = 2 * p + half
                    for s in range(STEPS):
                        i = 2 * STEPS * p + STEPS * half + s
                        act.wait_ge(scores_ready, i + 1)
                        if not (start and half == 0):
                            act.wait_ge(p_lo_ready, i - (RING - 1))
                        act.activation(pr32[:, s % RING, :], scores[s % 2][:, :], ACT.Exp,
                                       bias=boost[:, 0:1], scale=scale[:, 0:1]).then_inc(exp_done, 1)
                        if s == 1 and not (start and half == 0):
                            t_high(u - 1)
                        act.wait_ge(exp_done, i + 1)
                        if not (start and half == 0):
                            act.wait_ge(pv_done, i - (RING - 1))
                        act.activation(pr_hi[:, s % RING, :], pr32[:, s % RING, :], ACT.Copy)\
                           .then_inc(p_hi_ready, 1)
                        if s == 0 and (g0, g1)[half]:
                            g_high(misc[:, :], p + 1 + half, 1 - half, u + 3)

            for n, (first, last, *does) in enumerate(SEGMENTS):
                if last - first == 1:
                    pair(first, *does)
                else:
                    with act.Fori(first, last) as p:
                        pair(p, *does)
                if n == FFN_AT:
                    for e in range(E):
                        act.wait_ge(w1_turned, e + 1)
                        if e >= 2:
                            act.wait_ge(f_ps, e - 1)
                        act.activation(w1T[:, e % 2, :], max_ps[:, (e % 2) * 512:(e % 2) * 512 + M], ACT.Copy)\
                           .then_inc(w1_evacuated, 1)
            t_high(UNITS - 1)

        @block.tensor
        def _(pe):
            def three_pass(dst, lhs_hi, lhs_lo, rhs_hi, rhs_lo, start=True, stop=True):
                pe.matmul(dst, lhs_hi, rhs_hi, start=start, stop=False)
                pe.matmul(dst, lhs_hi, rhs_lo, start=False, stop=False)
                return pe.matmul(dst, lhs_lo, rhs_hi, start=False, stop=stop)

            pe.wait_ge(consts, 7)
            pe.wait_ge(kv_in, 32)
            for n in range(2):
                last = pe.matmul(t_ps[:, n * P:(n + 1) * P], wkv[:, n, :], centre[:, :], start=True, stop=True)
            last.then_inc(transposed, 1)
            pe.wait_ge(q_in, 16)
            for h in range(H):
                last = pe.matmul(scores[0][:, h * P:(h + 1) * P], wq_sb[:, h, :], centre[:, :], start=True, stop=True)
            last.then_inc(transposed, 1)
            pe.wait_ge(o_in, 16)
            for h in range(H):
                last = pe.matmul(scores[1][:, h * P:(h + 1) * P], wo_sb[:, h, :], ident[:, :], start=True, stop=True)
            last.then_inc(transposed, 1)

            pe.wait_ge(kv_ready, 1)
            pe.wait_ge(evacuated, 1)
            for h in range(H):
                last = pe.matmul(scores[0][:, h * P:(h + 1) * P], wqT[:, h, :], wkvT[:, 0:P], start=True, stop=True)
            last.then_inc(folded, 1)
            pe.wait_ge(evacuated, 2)
            for n in range(2):
                last = pe.matmul(scores[1][:, n * 512:(n + 1) * 512], wkvT[:, P:2 * P],
                                 woT[:, n * 512:(n + 1) * 512], start=True, stop=True)
            last.then_inc(folded, 1)

            for t in range(AHEAD):
                pe.wait_ge(xn_ready, t + 1)
                dst = (max16[:, t * 2 * P:(t + 1) * 2 * P] if t < NT else misc16[:, 0:2 * P])
                pe.transpose(dst[:, 0:P], xn_hi[:, t, :], ident16[:, :])
                last = pe.transpose(dst[:, P:2 * P], xn_lo[:, t, :], ident16[:, :])
                if t in (HT - 1, NT - 1, AHEAD - 1):
                    last.then_inc(xT_ps, 1)

            def batch_tile(pair):
                return (pair // H) * NT

            def project(dst, pair, half):
                tile = batch_tile(pair) + half * HT
                h = pair % H
                a_h, a_l = a_hi[:, bass.ds(h, 1), :], a_lo[:, bass.ds(h, 1), :]
                three_pass(dst, a_h, a_l, x_hi(tile, HT), x_lo(tile, HT)).then_inc(g_ps, 1)

            def max_tile(dst, pair, half, t):
                queries = g_slot(g_hi, pair, half, t * P, P)
                for n in range(2):
                    last = pe.matmul(dst[:, n * HALF:(n + 1) * HALF], queries,
                                     x_hi(batch_tile(pair) + n * HT, HT), start=True, stop=True)
                last.then_inc(max_scores, 1)

            def turn_max(unit, slot):
                pe.wait_ge(max_done, HT * (unit + 1))
                pe.transpose(misc16[0:HT, 0:P], row_max[:, slot, :], ident16[:, :]).then_inc(max_turned, 1)

            pe.wait_ge(weights_ready, 2)
            pe.wait_ge(xT_ready, AHEAD)
            for u, dst in enumerate((scores[0][:, 0:HALF], scores[0][:, HALF:2 * HALF], t_ps[:, :])):
                project(dst, u // 2, u % 2)
            for j in range(2 * HT):
                if j % HT == 0:
                    pe.wait_ge(g_hi_ready, j // HT + 1)
                if j >= 2:
                    pe.wait_ge(max_done, j - 1)
                max_tile((max_ps, scores[1])[j % 2], 0, j // HT, j % HT)
                if j == HT:
                    turn_max(0, 0)

            def weigh(k_pair, k_step, ring):
                tile = batch_tile(k_pair) + 2 * k_step
                for j in range(2):
                    first, last = k_step == 0 and j == 0, k_step == STEPS - 1 and j == 1
                    keys_hi, keys_lo = xn_hi[:, bass.ds(tile + j, 1), :], xn_lo[:, bass.ds(tile + j, 1), :]
                    p_hi, p_lo = pr_hi[:, ring, j * HALF:(j + 1) * HALF], pr_lo[:, ring, j * HALF:(j + 1) * HALF]
                    done = three_pass(t_ps[:, :], keys_hi, keys_lo, p_hi, p_lo, start=first, stop=last)
                done.then_inc(pv_done, 1)

            def head_out(pair, g):
                c_h, c_l = c_hi[:, bass.ds(pair % H, 1), :], c_lo[:, bass.ds(pair % H, 1), :]
                for q in range(2):
                    cols = slice((2 * g + q) * P, (2 * g + q + 1) * P)
                    last = three_pass(misc[:, q * 256:q * 256 + YW], t_hi[:, cols], t_lo[:, cols], c_h, c_l)
                last.then_inc(y_ps, 1)

            def ffn(dst, tile):
                return three_pass(dst, x_hi(tile), x_lo(tile), f_hi[:, :], f_lo[:, :])

            def pair(p, ln, finish, g0, g1, maxima):
                start = isinstance(p, int) and p == 0
                for half in range(2):
                    u = 2 * p + half
                    begun = not (start and half == 0)
                    before = p - 1 + half
                    has_g = (g0, g1)[half]
                    for s in range(STEPS):
                        i = 2 * STEPS * p + STEPS * half + s
                        if s == 0:
                            pe.wait_ge(max_landed, 16 * (u + 1))
                        if begun or s >= 2:
                            pe.wait_ge(exp_done, i - 1)
                        for j in range(2):
                            tile = batch_tile(p) + 2 * s + j
                            last = three_pass(scores[s % 2][:, j * HALF:(j + 1) * HALF], x_hi(tile), x_lo(tile),
                                              g_slot(g_hi, p, half), g_slot(g_lo, p, half))
                        last.then_inc(scores_ready, 1)

                        if s == 2 and (half == 0 or maxima):
                            if half == 0 and finish:
                                pe.wait_ge(tile_done, p - (H - 1))
                            elif half == 1 and ln:
                                pe.wait_ge(xT_ready, p + AHEAD + 1)
                            elif has_g:
                                pe.wait_ge(g_lo_ready, u + 4)
                            turn_max(u + 1, 1 - half)
                        if maxima:
                            if s == 0:
                                pe.wait_ge(g_hi_ready, u + 3)
                            pe.wait_ge(max_done, HT * (u + 2) + s)
                            max_tile(max_ps, p + 1, half, s)

                        if begun or s >= 2:
                            pe.wait_ge(p_lo_ready, i - 1)
                            if s == 2 and begun:
                                pe.wait_ge(t_lo_ready, u)
                            if s < 2:
                                weigh(before, s + 2, (s + 2) % RING)
                            else:
                                weigh(p, s - 2, (s + 2) % RING)

                        if s == 0 and has_g:
                            if begun and not (start and half == 1):
                                pe.wait_ge(y_added, 2 * u - 2)
                            else:
                                pe.wait_ge(max_negated, 1)
                            pe.wait_ge(xT_ready, p + AHEAD if ln else TILES)
                            project(misc[:, :], p + 1 + half, 1 - half)
                        if s == 1 and half == 0 and finish:
                            if has_g:
                                pe.wait_ge(g_lo_ready, u + 4)
                            else:
                                pe.wait_ge(y_added, 2 * u - 2)
                            pe.wait_ge(weights_ready, 3)
                            ffn(misc[:, 0:D], p - H).then_inc(ffn_ps, 1)
                        if s == 1 and half == 1 and ln:
                            pe.wait_ge(g_lo_ready, u + 4)
                            pe.wait_ge(xn_ready, p + AHEAD + 1)
                            pe.transpose(misc16[:, 0:P], xn_hi[:, bass.ds(p + AHEAD, 1), :], ident16[:, :])
                            pe.transpose(misc16[:, P:2 * P], xn_lo[:, bass.ds(p + AHEAD, 1), :], ident16[:, :])\
                              .then_inc(xT_ps, 1)
                        if s == 2 and begun:
                            if half == 0 or maxima:
                                pe.wait_ge(max_negated, u + 2)
                            head_out(before, 0)
                        if s == 3 and begun:
                            pe.wait_ge(y_added, 2 * u - 1)
                            head_out(before, 1)

            def fold_ffn():
                pe.wait_ge(ffn_in, 32)
                for e in range(E + 1):
                    if e < E:
                        if e == 0:
                            pe.wait_ge(max_done, HT * (2 * H + 2))
                        if e >= 2:
                            pe.wait_ge(w1_evacuated, e - 1)
                        for c in range(MC):
                            at = (e % 2) * 512 + c * P
                            last = pe.matmul(max_ps[:, at:at + P], w1_sb[:, e, c * P:(c + 1) * P],
                                             centre[:, :], start=True, stop=True)
                        last.then_inc(w1_turned, 1)
                    if e >= 1:
                        d = e - 1
                        if d == 0:
                            pe.wait_ge(y_added, 4 * H - 2)
                        pe.wait_ge(w1_evacuated, d + 1)
                        for c in range(MC):
                            last = pe.matmul(misc[:, 0:D], w1T[:, d % 2, c * P:(c + 1) * P], w2_sb[:, d, c, :],
                                             start=d == 0 and c == 0, stop=d == E - 1 and c == MC - 1)
                        last.then_inc(f_ps, 1)
                pe.wait_ge(f_copied, 1)

            for n, (first, last_pair, *does) in enumerate(SEGMENTS):
                if last_pair - first == 1:
                    pair(first, *does)
                else:
                    with pe.Fori(first, last_pair) as p:
                        pair(p, *does)
                if n == FFN_AT:
                    fold_ffn()

            for k in range(2):
                pe.wait_ge(p_lo_ready, STEPS * UNITS - 1 + k)
                weigh(PAIRS - 1, STEPS - 2 + k, (STEPS - 2 + k) % RING)
            pe.wait_ge(exp_done, STEPS * UNITS)
            for t in range(NT):
                last = ffn(scores[0][:, t * P:(t + 1) * P], TILES - NT + t)
            last.then_inc(ffn_ps, 1)
            pe.wait_ge(t_lo_ready, UNITS)
            pe.wait_ge(y_added, 2 * UNITS - 2)
            head_out(PAIRS - 1, 0)
            pe.wait_ge(y_added, 2 * UNITS - 1)
            head_out(PAIRS - 1, 1)

        @block.vector
        def _(dve):
            dve.memset(xn_hi[:, :, 0:1], 1.0).then_inc(slot_set, 1)
            dve.memset(xn_lo[:, :, 0:1], 0.0).then_inc(slot_set, 1)
            dve.memset(boost[:, :], LOG_BOOST).then_inc(slot_set, 1)
            dve.memset(c_hi[:, :, P:YW], 0.0).then_inc(slot_set, 1)
            dve.memset(c_lo[:, :, P:YW], 0.0).then_inc(slot_set, 1)
            dve.wait_ge(slot_set, 5)
            dve.memset(c_hi[0:1, :, P:P + 1], 1.0).then_inc(slot_set, 1)

            def tile_mean(slot):
                dve.bn_aggr(mean_var[:, slot, :], stats[:, slot, :]).then_inc(ln_mean, 1)

            def normalise(tile, slot, row):
                dve.tensor_scalar(xn32[:, row, 1:D], xacc[:, bass.ds(tile, 1), 1:D], mean_var[:, slot, 0:1],
                                  rstd[:, slot:slot + 1], ALU.subtract, ALU.mult).then_inc(ln_xn32, 1)

            def split_high(tile, tiles, count):
                dve.wait_ge(ln_xn32, count)
                dve.tensor_copy(xn_hi[:, bass.ds(tile, tiles), 1:D], xn32[:, 0:tiles, 1:D]).then_inc(ln_hi, tiles)

            def split_low(tile, tiles, count):
                dve.wait_ge(ln_hi, count)
                dve.tensor_tensor(xn_lo[:, bass.ds(tile, tiles), 1:D], xn32[:, 0:tiles, 1:D],
                                  xn_hi[:, bass.ds(tile, tiles), 1:D], ALU.subtract).then_inc(xn_ready, tiles)

            dve.wait_ge(transposed, 1)
            dve.tensor_copy(wkvT[:, :], t_ps[:, 0:2 * P]).then_inc(kv_ready, 1)
            dve.wait_ge(x_in, 16)
            for t in range(AHEAD):
                dve.bn_stats(stats[:, t, :], xacc[:, t, :]).then_inc(ln_stats, 1)
            for t in range(AHEAD):
                dve.wait_ge(ln_stats, t + 1)
                tile_mean(t)
            dve.wait_ge(ln_mean, AHEAD)
            dve.tensor_scalar_add(var_eps[:, 0:AHEAD], mean_var[:, 0:AHEAD, 1], EPS).then_inc(ln_var, 1)
            dve.wait_ge(ln_rstd, AHEAD)
            for t in range(AHEAD):
                normalise(t, t, t)
            split_high(0, AHEAD, AHEAD)
            split_low(0, AHEAD, AHEAD)
            dve.wait_ge(x_in2, 16)

            def power_of_two(n0, n1, done):
                dve.tensor_scalar_max(amax_floor[:, n0:n1], amax_all[:, n0:n1], TINY).then_inc(scales_a, 1)
                dve.wait_ge(scales_a, 2 * done + 1)
                dve.tensor_scalar(scale[:, n0:n1].bitcast(U32), amax_floor[:, n0:n1].bitcast(U32), EXPONENT, None,
                                  ALU.bitwise_and).then_inc(scales_a, 1)
                dve.wait_ge(scales_a, 2 * done + 2)
                dve.reciprocal(inv_scale[:, n0:n1], scale[:, n0:n1]).then_inc(scales, 1)
                dve.wait_ge(scales, done + 1)

            for n in range(2):
                dve.wait_ge(folded, n + 1)
                dve.tensor_reduce(amax[:, n:n + 1], scores[n][:, :], AX_X, ALU.max, apply_absolute_value=True)\
                   .then_inc(amax_ready, 1)
            for n in range(3):
                dve.wait_ge(xT_ps, n + 1)
                if n < 2:
                    src = max16[:, n * 2 * HALF:(n + 1) * 2 * HALF].rearrange("p (t k c) -> p k t c", k=2, c=P)
                    dst = xT[:, :, n * HALF:(n + 1) * HALF].rearrange("p k (t c) -> p k t c", c=P)
                    dve.tensor_copy(dst, src).then_inc(xT_ready, HT)
                else:
                    dve.tensor_copy(xT[:, :, NT * P:(NT + 1) * P], misc16[:, 0:2 * P].rearrange("p (k c) -> p k c", k=2))\
                       .then_inc(xT_ready, 1)
            dve.wait_ge(amax_spread, 1)
            power_of_two(0, 2, 0)
            for n, (hi, lo) in enumerate(((a_hi, a_lo), (c_hi, c_lo))):
                dve.wait_ge(hi_ready, n + 1)
                dve.scalar_tensor_tensor(out=lo[:, :, 0:P], in0=scores[n][:, :].rearrange("p (h k) -> p h k", h=H),
                                         scalar=inv_scale[:, n:n + 1], in1=hi[:, :, 0:P],
                                         op0=ALU.mult, op1=ALU.subtract).then_inc(weights_ready, 1)

            def g_low(source, pair, half, unit):
                dve.wait_ge(g_hi_ready, unit + 1)
                dve.tensor_tensor(g_slot(g_lo, pair, half), source, g_slot(g_hi, pair, half), ALU.subtract)\
                   .then_inc(g_lo_ready, 1)

            def take_max(source, unit, slot, t):
                dve.wait_ge(max_scores, HT * unit + t + 1)
                dve.reduce_max(row_max[:, slot, t:t + 1], source, AX_X).then_inc(max_done, 1)

            def negate_max(unit, slot):
                dve.wait_ge(max_turned, unit + 1)
                if not isinstance(unit, int) or unit >= 2:
                    dve.wait_ge(max_landed, 16 * (unit - 1))
                dve.tensor_scalar_mul(minus_max[:, slot, :], misc16[0:HT, 0:P], -1.0).then_inc(max_negated, 1)

            for j in range(2 * HT):
                take_max((max_ps, scores[1])[j % 2][:, :], j // HT, j // HT, j % HT)
                if j == HT - 1:
                    g_low(scores[0][:, 0:HALF], 0, 0, 0)
                if j == HT:
                    negate_max(0, 0)
                    g_low(scores[0][:, HALF:2 * HALF], 0, 1, 1)
                    g_low(t_ps[:, :], 1, 0, 2)

            def add_head(first_tile, g, count):
                dve.wait_ge(y_ps, count + 1)
                if not isinstance(count, int) or count > 0:
                    dve.wait_ge(y_added, count)
                dve.reciprocal(recip[:, :], misc[:, :].rearrange("p (q c) -> p q c", c=256)[:, :, P]).then_inc(y_recip, 1)
                dve.wait_ge(y_recip, count + 1)
                dve.tensor_scalar(recip_c[:, :], recip[:, :], scale[:, 1:2], None, ALU.mult).then_inc(y_recip_c, 1)
                dve.wait_ge(y_recip_c, count + 1)
                for q in range(2):
                    acc = xacc[:, bass.ds(first_tile + (2 * g + q), 1), :]
                    last = dve.scalar_tensor_tensor(out=acc, in0=misc[:, q * 256:q * 256 + D], scalar=recip_c[:, q:q + 1],
                                                    in1=acc, op0=ALU.mult, op1=ALU.add)
                last.then_inc(y_added, 1)

            def pair(p, ln, finish, g0, g1, maxima):
                start = isinstance(p, int) and p == 0
                for half in range(2):
                    u = 2 * p + half
                    begun = not (start and half == 0)
                    before = ((p - 1 + half) // H) * NT + (1 - half) * HT
                    for s in range(STEPS):
                        ahead = ln and half == 0
                        if s == 1 and (g0, g1)[half]:
                            g_low(misc[:, :], p + 1 + half, 1 - half, u + 3)
                        if s == 2 and (half == 0 or maxima):
                            negate_max(u + 1, 1 - half)
                        if s == 1 and ahead:
                            dve.wait_ge(ln_stats, p + AHEAD + 1)
                        if maxima:
                            take_max(max_ps[:, :], u + 2, half, s)
                        if s == 0 and ahead:
                            dve.wait_ge(ln_mean, p + AHEAD)
                            dve.bn_stats(stats[:, AHEAD, :], xacc[:, bass.ds(p + AHEAD, 1), :]).then_inc(ln_stats, 1)
                        if s == 1 and ahead:
                            tile_mean(AHEAD)
                        if s == 1 and half == 0 and finish:
                            dve.wait_ge(ffn_ps, p - (H - 1))
                            dve.wait_ge(y_added, 2 * u - 2)
                            tile = xacc[:, bass.ds(p - H, 1), :]
                            dve.scalar_tensor_tensor(out=tile, in0=misc[:, 0:D], scalar=scale[:, 2:3], in1=tile,
                                                     op0=ALU.mult, op1=ALU.add).then_inc(tile_done, 1)
                        if s == 1 and half == 1 and ln:
                            dve.wait_ge(xT_ps, p + 4)
                            dve.tensor_copy(xT[:, :, bass.ds((p + AHEAD) * P, P)],
                                            misc16[:, 0:2 * P].rearrange("p (k c) -> p k c", k=2)).then_inc(xT_ready, 1)
                        if s == 1 and begun:
                            dve.wait_ge(t_hi_ready, u)
                            dve.tensor_tensor(t_lo[:, :], t_ps[:, :], t_hi[:, :], ALU.subtract).then_inc(t_lo_ready, 1)
                        if s == 1 and ahead:
                            dve.wait_ge(ln_mean, p + AHEAD + 1)
                            dve.tensor_scalar_add(var_eps[:, AHEAD:AHEAD + 1], mean_var[:, AHEAD, 1:2], EPS)\
                               .then_inc(ln_var, 1)
                        if s == 2 and begun:
                            add_head(before, 0, 2 * u - 2)
                        if s == 3 and begun:
                            add_head(before, 1, 2 * u - 1)
                        if s == 3 and ahead:
                            dve.wait_ge(ln_rstd, p + AHEAD + 1)
                            dve.wait_ge(xn_ready, p + AHEAD)
                            normalise(p + AHEAD, AHEAD, 0)
                            split_high(p + AHEAD, 1, p + AHEAD + 1)
                        if s == 0 and half == 1 and ln:
                            split_low(p + AHEAD, 1, p + AHEAD + 1)

            for n, (first, last_pair, *does) in enumerate(SEGMENTS):
                if last_pair - first == 1:
                    pair(first, *does)
                else:
                    with dve.Fori(first, last_pair) as p:
                        pair(p, *does)
                if n == FFN_AT:
                    dve.wait_ge(f_ps, E)
                    dve.tensor_copy(f32w[:, :], misc[:, 0:D]).then_inc(f_copied, 1)
                    dve.wait_ge(f_copied, 1)
                    dve.tensor_reduce(amax[:, 2:3], f32w[:, :], AX_X, ALU.max, apply_absolute_value=True)\
                       .then_inc(amax_ready, 1)
                    dve.wait_ge(amax_spread, 2)
                    power_of_two(2, 3, 1)
                    dve.tensor_scalar(f_hi[:, :], f32w[:, :], inv_scale[:, 2:3], None, ALU.mult).then_inc(hi_ready, 1)
                    dve.wait_ge(hi_ready, 3)
                    dve.scalar_tensor_tensor(out=f_lo[:, :], in0=f32w[:, :], scalar=inv_scale[:, 2:3], in1=f_hi[:, :],
                                             op0=ALU.mult, op1=ALU.subtract).then_inc(weights_ready, 1)

            dve.wait_ge(t_hi_ready, UNITS)
            dve.tensor_tensor(t_lo[:, :], t_ps[:, :], t_hi[:, :], ALU.subtract).then_inc(t_lo_ready, 1)
            dve.wait_ge(ffn_ps, PAIRS - H + 1)
            dve.wait_ge(y_added, 2 * UNITS - 2)
            tiles = xacc[:, TILES - NT:TILES, :]
            dve.scalar_tensor_tensor(out=tiles, in0=scores[0][:, :].rearrange("p (t d) -> p t d", d=D),
                                     scalar=scale[:, 2:3], in1=tiles, op0=ALU.mult, op1=ALU.add).then_inc(tile_done, 1)
            dve.wait_ge(tile_done, PAIRS - H + 1)
            for g in range(2):
                add_head(TILES - HT, g, 2 * UNITS - 2 + g)


_INS = ['L0_attn_x', 'L0_attn_proj_q', 'L0_attn_proj_k', 'L0_attn_proj_v', 'L0_attn_proj_o', 'L0_ffn_w1', 'L0_ffn_w2']


def kernel(**inputs):
    import numpy as _np
    import concourse.bacc as _bacc
    from concourse import mybir as _mybir
    from concourse.bass_utils import run_bass_kernel_spmd as _run

    nc = _bacc.Bacc("TRN2", target_bir_lowering=False, num_devices=1)
    arrays, args = {}, []
    for name in _INS:
        a = _np.ascontiguousarray(inputs[name])
        arrays[f"in_{name}_dram"] = a
        args.append(nc.dram_tensor(f"in_{name}_dram", a.shape, _mybir.dt.from_np(a.dtype), kind="ExternalInput").ap())
    shape = inputs['L0_attn_x'].shape
    args.append(nc.dram_tensor("out_0_dram", shape, _mybir.dt.float32, kind="ExternalOutput").ap())
    attention_ffn(nc, *args)
    r = _run(nc, [arrays], core_ids=[0])
    return r.results[0]["out_0_dram"]
```
